# Optimizing a Trainium2 kernel written in Bass

```python
import numpy as np
import jax
import jax.numpy as jnp

def _softmax(x, axis=-1):
    return jax.nn.softmax(x, axis=axis)

def _gelu(x):
    return jax.nn.gelu(x, approximate=True)

def _silu(x):
    return jax.nn.silu(x)

def _sigmoid(x):
    return jax.nn.sigmoid(x)

def _layernorm(x, axis=-1, eps=1e-05):
    m = jnp.mean(x, axis=axis, keepdims=True)
    v = jnp.var(x, axis=axis, keepdims=True)
    return (x - m) / jnp.sqrt(v + eps)

def _scatter_add(tgt, idx, src, axis=0):
    return tgt.at[idx].add(src)

def _segment_sum(src, seg, n):
    return jax.ops.segment_sum(src, seg, n)
kernel_name = 'mk_adaln_d2_jaxref_r8_3477c4'

def setup_inputs(seed: int=0):
    np.random.seed(seed)
    _w = jnp.asarray

    def _L0_attn_setup():
        import jax, jax.numpy as jnp
        import numpy as np
        from jax import lax
        HIDDEN = 128
        HEADS = 8
        HEAD_DIM = HIDDEN // HEADS
        B, S = (2, 256)
        NORADRENALINE = 0.5
        DOPAMINE = 0.8
        key = jax.random.key(seed)
        ks = jax.random.split(key, 12)
        std = 0.02
        return {'x': jax.random.normal(ks[0], (B, S, HIDDEN), dtype=jnp.float32), 'Wq': jax.random.normal(ks[1], (HIDDEN, HIDDEN), dtype=jnp.float32) * std, 'bq': jnp.zeros((HIDDEN,), dtype=jnp.float32), 'Wk': jax.random.normal(ks[2], (HIDDEN, HIDDEN), dtype=jnp.float32) * std, 'bk': jnp.zeros((HIDDEN,), dtype=jnp.float32), 'Wv': jax.random.normal(ks[3], (HIDDEN, HIDDEN), dtype=jnp.float32) * std, 'bv': jnp.zeros((HIDDEN,), dtype=jnp.float32), 'Wo': jax.random.normal(ks[4], (HIDDEN, HIDDEN), dtype=jnp.float32) * std, 'bo': jnp.zeros((HIDDEN,), dtype=jnp.float32), 'conv_w': jax.random.normal(ks[5], (HEADS, 1, 3), dtype=jnp.float32) * 0.3, 'conv_b': jax.random.normal(ks[6], (HEADS,), dtype=jnp.float32) * 0.1}
    _L0_attn_in = _L0_attn_setup()

    def _L0_ffn_setup():
        import jax, jax.numpy as jnp
        import numpy as np
        TOP_K = 2
        EPS = 1e-05

        def layer_norm(x, g, b):
            mu = jnp.mean(x, axis=-1, keepdims=True)
            var = jnp.mean(jnp.square(x - mu), axis=-1, keepdims=True)
            return (x - mu) * jax.lax.rsqrt(var + EPS) * g + b
        key = jax.random.key(seed)
        ks = jax.random.split(key, 12)
        B, S, D, F, E = (2, 256, 128, 512, 8)
        std = 0.02
        return {'x': jax.random.normal(ks[0], (B, S, D), jnp.float32), 'g1': jnp.ones((D,), jnp.float32), 'be1': jnp.zeros((D,), jnp.float32), 'mix_w': jax.random.normal(ks[1], (D, D), jnp.float32) * std, 'mix_b': jnp.zeros((D,), jnp.float32), 'g2': jnp.ones((D,), jnp.float32), 'be2': jnp.zeros((D,), jnp.float32), 'router_w': jax.random.normal(ks[2], (D, E), jnp.float32) * std, 'w1': jax.random.normal(ks[3], (E, D, F), jnp.float32) * std, 'b1': jnp.zeros((E, F), jnp.float32), 'w2': jax.random.normal(ks[4], (E, F, D), jnp.float32) * std, 'b2': jnp.zeros((E, D), jnp.float32)}
    _L0_ffn_in = _L0_ffn_setup()
    _L0_c = _w((lambda *s: np.random.randn(*s).astype(np.float32) * 0.05)(8, 128))
    _L0_wmod = _w((lambda *s: np.random.randn(*s).astype(np.float32) * 0.05)(128, 6 * 128) * 128 ** (-0.5))

    def _L1_attn_setup():
        import math
        import jax, jax.numpy as jnp
        import numpy as np
        D_MODEL = 128
        D_STATE = 16
        D_CONV = 4
        EXPAND = 2
        D_INNER = D_MODEL * EXPAND
        B_SZ = 2
        L_SEQ = 256
        DT_MIN = 0.001
        DT_MAX = 0.1

        def _silu(v):
            return v * jax.nn.sigmoid(v)

        def _mamba(x, in_proj_w, conv_w, conv_b, x_proj_w, dt_proj_w, dt_proj_b, A_log, D, out_proj_w):
            xz = jnp.einsum('bld,ed->ble', x, in_proj_w)
            x_in, z = jnp.split(xz, 2, axis=-1)
            xc = jnp.swapaxes(x_in, 1, 2)
            xc = jax.lax.conv_general_dilated(xc, conv_w, window_strides=(1,), padding=[(D_CONV - 1, 0)], dimension_numbers=('NCH', 'OIH', 'NCH'), feature_group_count=D_INNER)
            xc = xc + conv_b[None, :, None]
            x_in = _silu(jnp.swapaxes(xc, 1, 2))
            dbc = jnp.einsum('bld,ed->ble', x_in, x_proj_w)
            delta_in = dbc[..., :D_INNER]
            Bp = dbc[..., D_INNER:D_INNER + D_STATE]
            Cp = dbc[..., D_INNER + D_STATE:]
            delta = jax.nn.softplus(jnp.einsum('bld,ed->ble', delta_in, dt_proj_w) + dt_proj_b)
            A = -jnp.exp(A_log)

            def step(h, inp):
                dt, bt, ct, xt = inp
                dA = jnp.exp(dt[:, :, None] * A[None])
                h = dA * h + dt[:, :, None] * bt[:, None, :] * xt[:, :, None]
                y = jnp.einsum('bds,bs->bd', h, ct) + D * xt
                return (h, y)
            tm = lambda a: jnp.swapaxes(a, 0, 1)
            h0 = jnp.zeros((x.shape[0], D_INNER, D_STATE), x.dtype)
            _, y = jax.lax.scan(step, h0, (tm(delta), tm(Bp), tm(Cp), tm(x_in)))
            y = jnp.swapaxes(y, 0, 1)
            return jnp.einsum('ble,de->bld', y * _silu(z), out_proj_w)
        key = jax.random.key(seed)
        ks = jax.random.split(key, 8)

        def lin(k, out_f, in_f):
            return jax.random.normal(k, (out_f, in_f), jnp.float32) / np.sqrt(in_f)
        x = jax.random.normal(ks[0], (B_SZ, L_SEQ, D_MODEL), jnp.float32)
        in_proj_w = lin(ks[1], 2 * D_INNER, D_MODEL)
        conv_w = jax.random.normal(ks[2], (D_INNER, 1, D_CONV), jnp.float32) / np.sqrt(D_CONV)
        conv_b = jnp.zeros((D_INNER,), jnp.float32)
        x_proj_w = lin(ks[3], 2 * D_STATE + D_INNER, D_INNER)
        dt_proj_w = lin(ks[4], D_INNER, D_INNER)
        dt = jnp.exp(jax.random.uniform(ks[5], (D_INNER,), jnp.float32) * (math.log(DT_MAX) - math.log(DT_MIN)) + math.log(DT_MIN))
        dt_proj_b = dt + jnp.log(-jnp.expm1(-dt))
        A_log = jnp.log(jnp.tile(jnp.arange(1, D_STATE + 1, dtype=jnp.float32), (D_INNER, 1)))
        D = jnp.ones((D_INNER,), jnp.float32)
        out_proj_w = lin(ks[6], D_MODEL, D_INNER)
        return dict(x=x, in_proj_w=in_proj_w, conv_w=conv_w, conv_b=conv_b, x_proj_w=x_proj_w, dt_proj_w=dt_proj_w, dt_proj_b=dt_proj_b, A_log=A_log, D=D, out_proj_w=out_proj_w)
    _L1_attn_in = _L1_attn_setup()

    def _L1_ffn_setup():
        import jax, jax.numpy as jnp
        import numpy as np
        B, T, C = (8, 256, 128)
        H = 512
        E = 8
        K = 2
        LOAD_FACTOR = 1.2
        N_LAYER = 12

        def _get_expert_inputs(x, logits, expert_capacity):
            Tt = logits.shape[0]
            Cc = x.shape[1]
            top_k_logits, expert_indices = jax.lax.top_k(logits, K)
            expert_probs = jax.nn.softmax(top_k_logits, axis=-1)
            ei = jnp.swapaxes(expert_indices, 0, 1).ravel()
            one_hot = jax.nn.one_hot(ei, E, dtype=jnp.int32)
            pos = jnp.cumsum(one_hot, axis=0) * one_hot - 1
            pos = pos.reshape(-1, Tt, E)
            pos = jnp.swapaxes(pos, 0, 1)
            pos = jnp.max(pos, axis=2)
            ei = jnp.swapaxes(ei.reshape(-1, Tt), 0, 1)
            buf = jnp.zeros((E, expert_capacity, Cc), x.dtype)
            xr = jnp.repeat(x, K, axis=0)
            expert_inputs = buf.at[ei.ravel(), pos.ravel()].add(xr)
            return (expert_probs, pos, ei, expert_inputs)
        key = jax.random.key(seed)
        ks = jax.random.split(key, 9)
        std = 0.02
        proj_std = 0.02 * (2 * N_LAYER) ** (-0.5)
        return {'x': jax.random.normal(ks[0], (B, T, C), jnp.float32), 'router_w': jax.random.normal(ks[1], (C, E), jnp.float32) * std, 'router_b': jnp.zeros((E,), jnp.float32), 'w_c_fc': jax.random.normal(ks[2], (E, C, H), jnp.float32) * std, 'b_c_fc': jnp.zeros((E, 1, H), jnp.float32), 'w_gate': jax.random.normal(ks[3], (E, C, H), jnp.float32) * std, 'b_gate': jnp.zeros((E, 1, H), jnp.float32), 'w_c_proj': jax.random.normal(ks[4], (E, H, C), jnp.float32) * proj_std, 'b_c_proj': jnp.zeros((E, 1, C), jnp.float32)}
    _L1_ffn_in = _L1_ffn_setup()
    _L1_c = _w((lambda *s: np.random.randn(*s).astype(np.float32) * 0.05)(8, 128))
    _L1_wmod = _w((lambda *s: np.random.randn(*s).astype(np.float32) * 0.05)(128, 6 * 128) * 128 ** (-0.5))
    _d = {'L0_attn_x': _L0_attn_in['x'], 'L0_attn_Wq': _L0_attn_in['Wq'], 'L0_attn_bq': _L0_attn_in['bq'], 'L0_attn_Wk': _L0_attn_in['Wk'], 'L0_attn_bk': _L0_attn_in['bk'], 'L0_attn_Wv': _L0_attn_in['Wv'], 'L0_attn_bv': _L0_attn_in['bv'], 'L0_attn_Wo': _L0_attn_in['Wo'], 'L0_attn_bo': _L0_attn_in['bo'], 'L0_attn_conv_w': _L0_attn_in['conv_w'], 'L0_attn_conv_b': _L0_attn_in['conv_b'], 'L0_ffn_g1': _L0_ffn_in['g1'], 'L0_ffn_be1': _L0_ffn_in['be1'], 'L0_ffn_mix_w': _L0_ffn_in['mix_w'], 'L0_ffn_mix_b': _L0_ffn_in['mix_b'], 'L0_ffn_g2': _L0_ffn_in['g2'], 'L0_ffn_be2': _L0_ffn_in['be2'], 'L0_ffn_router_w': _L0_ffn_in['router_w'], 'L0_ffn_w1': _L0_ffn_in['w1'], 'L0_ffn_b1': _L0_ffn_in['b1'], 'L0_ffn_w2': _L0_ffn_in['w2'], 'L0_ffn_b2': _L0_ffn_in['b2'], 'L0_c': _L0_c, 'L0_wmod': _L0_wmod, 'L1_attn_in_proj_w': _L1_attn_in['in_proj_w'], 'L1_attn_conv_w': _L1_attn_in['conv_w'], 'L1_attn_conv_b': _L1_attn_in['conv_b'], 'L1_attn_x_proj_w': _L1_attn_in['x_proj_w'], 'L1_attn_dt_proj_w': _L1_attn_in['dt_proj_w'], 'L1_attn_dt_proj_b': _L1_attn_in['dt_proj_b'], 'L1_attn_A_log': _L1_attn_in['A_log'], 'L1_attn_D': _L1_attn_in['D'], 'L1_attn_out_proj_w': _L1_attn_in['out_proj_w'], 'L1_ffn_router_w': _L1_ffn_in['router_w'], 'L1_ffn_router_b': _L1_ffn_in['router_b'], 'L1_ffn_w_c_fc': _L1_ffn_in['w_c_fc'], 'L1_ffn_b_c_fc': _L1_ffn_in['b_c_fc'], 'L1_ffn_w_gate': _L1_ffn_in['w_gate'], 'L1_ffn_b_gate': _L1_ffn_in['b_gate'], 'L1_ffn_w_c_proj': _L1_ffn_in['w_c_proj'], 'L1_ffn_b_c_proj': _L1_ffn_in['b_c_proj'], 'L1_c': _L1_c, 'L1_wmod': _L1_wmod}
    _x0 = _d['L0_attn_x']
    _d['L0_attn_x'] = jax.random.normal(jax.random.fold_in(jax.random.key(seed), 1), (8, 512, 128), dtype=_x0.dtype)
    del _x0
    return _d

def reference(L0_attn_x, L0_attn_Wq, L0_attn_bq, L0_attn_Wk, L0_attn_bk, L0_attn_Wv, L0_attn_bv, L0_attn_Wo, L0_attn_bo, L0_attn_conv_w, L0_attn_conv_b, L0_ffn_g1, L0_ffn_be1, L0_ffn_mix_w, L0_ffn_mix_b, L0_ffn_g2, L0_ffn_be2, L0_ffn_router_w, L0_ffn_w1, L0_ffn_b1, L0_ffn_w2, L0_ffn_b2, L0_c, L0_wmod, L1_attn_in_proj_w, L1_attn_conv_w, L1_attn_conv_b, L1_attn_x_proj_w, L1_attn_dt_proj_w, L1_attn_dt_proj_b, L1_attn_A_log, L1_attn_D, L1_attn_out_proj_w, L1_ffn_router_w, L1_ffn_router_b, L1_ffn_w_c_fc, L1_ffn_b_c_fc, L1_ffn_w_gate, L1_ffn_b_gate, L1_ffn_w_c_proj, L1_ffn_b_c_proj, L1_c, L1_wmod):

    def _L0_attn_ref(x, Wq, bq, Wk, bk, Wv, bv, Wo, bo, conv_w, conv_b):
        import jax, jax.numpy as jnp
        import numpy as np
        from jax import lax
        HIDDEN = 128
        HEADS = 8
        HEAD_DIM = HIDDEN // HEADS
        B, S = (2, 256)
        NORADRENALINE = 0.5
        DOPAMINE = 0.8
        b, s, h = x.shape
        scale = 1.0 / np.sqrt(HEAD_DIM)

        def heads(t):
            return t.reshape(b, s, HEADS, HEAD_DIM).transpose(0, 2, 1, 3)
        q = heads(x @ Wq + bq)
        k = heads(x @ Wk + bk)
        v = heads(x @ Wv + bv)
        scores = jnp.einsum('bhqd,bhkd->bhqk', q, k) * scale
        scores = scores * (1.0 + 0.5 * NORADRENALINE)
        top_k = max(1, int(s * 0.2))
        top_scores = lax.top_k(scores, top_k)[0]
        threshold = top_scores[..., -1:]
        emphasis = jnp.where(scores >= threshold, 1.0 + 0.3 * DOPAMINE, 1.0)
        scores = scores * emphasis
        scores_pooled = scores.mean(axis=-2)
        li = lax.conv_general_dilated(scores_pooled, conv_w, window_strides=(1,), padding=[(1, 1)], dimension_numbers=('NCH', 'OIH', 'NCH'), feature_group_count=HEADS) + conv_b[None, :, None]
        scores = scores * li[:, :, None, :]
        probs = jax.nn.softmax(scores, axis=-1)
        ctx = jnp.einsum('bhqk,bhkd->bhqd', probs, v)
        ctx = ctx.transpose(0, 2, 1, 3).reshape(b, s, h)
        return ctx @ Wo + bo

    def _L0_ffn_ref(x, g1, be1, mix_w, mix_b, g2, be2, router_w, w1, b1, w2, b2):
        import jax, jax.numpy as jnp
        import numpy as np
        TOP_K = 2
        EPS = 1e-05

        def layer_norm(x, g, b):
            mu = jnp.mean(x, axis=-1, keepdims=True)
            var = jnp.mean(jnp.square(x - mu), axis=-1, keepdims=True)
            return (x - mu) * jax.lax.rsqrt(var + EPS) * g + b
        res = x
        n = layer_norm(x, g1, be1)
        x = res + n + (n @ mix_w + mix_b)
        res = x
        n = layer_norm(x, g2, be2)
        B, S, D = n.shape
        E = w1.shape[0]
        flat = n.reshape(-1, D)
        probs = jax.nn.softmax(flat @ router_w, axis=-1)
        topw, topi = jax.lax.top_k(probs, TOP_K)
        combine = jnp.sum(jax.nn.one_hot(topi, E, dtype=flat.dtype) * topw[..., None], axis=1)
        h = jax.nn.silu(jnp.einsum('td,edf->tef', flat, w1) + b1)
        y = jnp.einsum('tef,efd->ted', h, w2) + b2
        out = jnp.einsum('te,ted->td', combine, y)
        return res + out.reshape(B, S, D)

    def _L1_attn_ref(x, in_proj_w, conv_w, conv_b, x_proj_w, dt_proj_w, dt_proj_b, A_log, D, out_proj_w):
        import math
        import jax, jax.numpy as jnp
        import numpy as np
        D_MODEL = 128
        D_STATE = 16
        D_CONV = 4
        EXPAND = 2
        D_INNER = D_MODEL * EXPAND
        B_SZ = 2
        L_SEQ = 256
        DT_MIN = 0.001
        DT_MAX = 0.1

        def _silu(v):
            return v * jax.nn.sigmoid(v)

        def _mamba(x, in_proj_w, conv_w, conv_b, x_proj_w, dt_proj_w, dt_proj_b, A_log, D, out_proj_w):
            xz = jnp.einsum('bld,ed->ble', x, in_proj_w)
            x_in, z = jnp.split(xz, 2, axis=-1)
            xc = jnp.swapaxes(x_in, 1, 2)
            xc = jax.lax.conv_general_dilated(xc, conv_w, window_strides=(1,), padding=[(D_CONV - 1, 0)], dimension_numbers=('NCH', 'OIH', 'NCH'), feature_group_count=D_INNER)
            xc = xc + conv_b[None, :, None]
            x_in = _silu(jnp.swapaxes(xc, 1, 2))
            dbc = jnp.einsum('bld,ed->ble', x_in, x_proj_w)
            delta_in = dbc[..., :D_INNER]
            Bp = dbc[..., D_INNER:D_INNER + D_STATE]
            Cp = dbc[..., D_INNER + D_STATE:]
            delta = jax.nn.softplus(jnp.einsum('bld,ed->ble', delta_in, dt_proj_w) + dt_proj_b)
            A = -jnp.exp(A_log)

            def step(h, inp):
                dt, bt, ct, xt = inp
                dA = jnp.exp(dt[:, :, None] * A[None])
                h = dA * h + dt[:, :, None] * bt[:, None, :] * xt[:, :, None]
                y = jnp.einsum('bds,bs->bd', h, ct) + D * xt
                return (h, y)
            tm = lambda a: jnp.swapaxes(a, 0, 1)
            h0 = jnp.zeros((x.shape[0], D_INNER, D_STATE), x.dtype)
            _, y = jax.lax.scan(step, h0, (tm(delta), tm(Bp), tm(Cp), tm(x_in)))
            y = jnp.swapaxes(y, 0, 1)
            return jnp.einsum('ble,de->bld', y * _silu(z), out_proj_w)
        return _mamba(x, in_proj_w, conv_w, conv_b, x_proj_w, dt_proj_w, dt_proj_b, A_log, D, out_proj_w)

    def _L1_ffn_ref(x, router_w, router_b, w_c_fc, b_c_fc, w_gate, b_gate, w_c_proj, b_c_proj):
        import jax, jax.numpy as jnp
        import numpy as np
        B, T, C = (8, 256, 128)
        H = 512
        E = 8
        K = 2
        LOAD_FACTOR = 1.2
        N_LAYER = 12

        def _get_expert_inputs(x, logits, expert_capacity):
            Tt = logits.shape[0]
            Cc = x.shape[1]
            top_k_logits, expert_indices = jax.lax.top_k(logits, K)
            expert_probs = jax.nn.softmax(top_k_logits, axis=-1)
            ei = jnp.swapaxes(expert_indices, 0, 1).ravel()
            one_hot = jax.nn.one_hot(ei, E, dtype=jnp.int32)
            pos = jnp.cumsum(one_hot, axis=0) * one_hot - 1
            pos = pos.reshape(-1, Tt, E)
            pos = jnp.swapaxes(pos, 0, 1)
            pos = jnp.max(pos, axis=2)
            ei = jnp.swapaxes(ei.reshape(-1, Tt), 0, 1)
            buf = jnp.zeros((E, expert_capacity, Cc), x.dtype)
            xr = jnp.repeat(x, K, axis=0)
            expert_inputs = buf.at[ei.ravel(), pos.ravel()].add(xr)
            return (expert_probs, pos, ei, expert_inputs)
        Bb, Tt, Cc = x.shape
        logits = jnp.einsum('btc,ce->bte', x, router_w) + router_b
        cap = int(LOAD_FACTOR * K * Tt // E)
        probs, pos, idx, einp = jax.vmap(lambda xb, lb: _get_expert_inputs(xb, lb, cap))(x, logits)
        if Bb % E == 0:
            t = einp.reshape(E, Bb // E, E, cap, Cc)
            t = jnp.swapaxes(t, 0, 2)
        else:
            t = jnp.swapaxes(einp, 0, 1)
        einp2 = t.reshape(E, Bb * cap, Cc)
        h = jnp.einsum('eti,eih->eth', einp2, w_c_fc) + b_c_fc
        g = jnp.einsum('eti,eih->eth', einp2, w_gate) + b_gate
        o = jnp.einsum('eth,eho->eto', jax.nn.silu(h * g), w_c_proj) + b_c_proj
        if Bb % E == 0:
            o = o.reshape(E, Bb // E, E, cap, Cc)
            o = jnp.swapaxes(o, 0, 2)
            o = o.reshape(Bb, E, cap, Cc)
        else:
            o = o.reshape(E, Bb, cap, Cc)
            o = jnp.swapaxes(o, 0, 1)

        def collect(eo, i, p, pr):
            sel = eo[i, p]
            return jnp.sum(pr[..., None] * sel, axis=1)
        return jax.vmap(collect)(o, idx, pos, probs)
    x = L0_attn_x
    mod = (_silu(L0_c) @ L0_wmod).reshape(L0_c.shape[0], 6, 1, -1)
    sa, ca, ga, sb, cb, gb = (mod[:, 0], mod[:, 1], mod[:, 2], mod[:, 3], mod[:, 4], mod[:, 5])
    ga = (2 * (ga >= 0) - 1) * jnp.maximum(jnp.abs(ga), 0.25)
    gb = (2 * (gb >= 0) - 1) * jnp.maximum(jnp.abs(gb), 0.25)
    h = _layernorm(x, axis=-1) * (1 + ca) + sa
    x = x + ga * _L0_attn_ref(h, L0_attn_Wq, L0_attn_bq, L0_attn_Wk, L0_attn_bk, L0_attn_Wv, L0_attn_bv, L0_attn_Wo, L0_attn_bo, L0_attn_conv_w, L0_attn_conv_b)
    h = _layernorm(x, axis=-1) * (1 + cb) + sb
    x = x + gb * _L0_ffn_ref(h, L0_ffn_g1, L0_ffn_be1, L0_ffn_mix_w, L0_ffn_mix_b, L0_ffn_g2, L0_ffn_be2, L0_ffn_router_w, L0_ffn_w1, L0_ffn_b1, L0_ffn_w2, L0_ffn_b2)
    mod = (_silu(L1_c) @ L1_wmod).reshape(L1_c.shape[0], 6, 1, -1)
    sa, ca, ga, sb, cb, gb = (mod[:, 0], mod[:, 1], mod[:, 2], mod[:, 3], mod[:, 4], mod[:, 5])
    ga = (2 * (ga >= 0) - 1) * jnp.maximum(jnp.abs(ga), 0.25)
    gb = (2 * (gb >= 0) - 1) * jnp.maximum(jnp.abs(gb), 0.25)
    h = _layernorm(x, axis=-1) * (1 + ca) + sa
    x = x + ga * _L1_attn_ref(h, L1_attn_in_proj_w, L1_attn_conv_w, L1_attn_conv_b, L1_attn_x_proj_w, L1_attn_dt_proj_w, L1_attn_dt_proj_b, L1_attn_A_log, L1_attn_D, L1_attn_out_proj_w)
    h = _layernorm(x, axis=-1) * (1 + cb) + sb
    x = x + gb * _L1_ffn_ref(h, L1_ffn_router_w, L1_ffn_router_b, L1_ffn_w_c_fc, L1_ffn_b_c_fc, L1_ffn_w_gate, L1_ffn_b_gate, L1_ffn_w_c_proj, L1_ffn_b_c_proj)
    return x

_drawn_inputs = setup_inputs


def setup_inputs(seed=0):
    import zlib

    import numpy as np

    out = dict(_drawn_inputs(seed))
    spreads = {'L0_attn_bq': (0.0, 0.8),
     'L0_attn_bk': (0.0, 0.8),
     'L0_attn_bv': (0.0, 0.8),
     'L0_attn_bo': (0.0, 0.322),
     'L0_ffn_g1': (1.0, 0.2),
     'L0_ffn_be1': (0.0, 0.314),
     'L0_ffn_mix_b': (0.0, 0.34),
     'L0_ffn_g2': (1.0, 0.6),
     'L0_ffn_be2': (0.0, 0.8),
     'L0_ffn_b1': (0.0, 0.8),
     'L0_ffn_b2': (0.0, 0.8),
     'L1_attn_conv_b': (0.0, 0.8),
     'L1_attn_D': (1.0, 0.6),
     'L1_ffn_router_b': (0.0, 2.0),
     'L1_ffn_b_c_fc': (0.0, 2.0),
     'L1_ffn_b_gate': (0.0, 2.0),
     'L1_ffn_b_c_proj': (0.0, 2.0)}
    factors = {'L0_attn_Wq': 8.0,
     'L0_attn_Wk': 8.0,
     'L0_attn_Wv': 8.0,
     'L0_attn_Wo': 8.0,
     'L0_attn_conv_w': 8.0,
     'L0_attn_conv_b': 8.0,
     'L0_ffn_router_w': 8.0,
     'L0_ffn_w1': 8.0,
     'L0_ffn_w2': 8.0,
     'L1_attn_x_proj_w': 3.206,
     'L1_attn_dt_proj_w': 6.367,
     'L1_attn_dt_proj_b': 5.501,
     'L1_attn_A_log': 5.7,
     'L1_ffn_router_w': 11.776,
     'L1_ffn_w_c_fc': 26.232,
     'L1_ffn_w_gate': 26.402,
     'L1_ffn_w_c_proj': 8.0}
    for name, (base, spread) in spreads.items():
        noise = np.random.default_rng([zlib.crc32(name.encode()), seed]).standard_normal(out[name].shape)
        drawn = base * np.exp(spread * noise) if base else spread * noise
        out[name] = jnp.asarray(drawn.astype(out[name].dtype))
    for name, factor in factors.items():
        out[name] = (out[name] * factor).astype(out[name].dtype)
    return out
```

```python
from contextlib import ExitStack, contextmanager

import numpy as np
import concourse.bass as bass
from concourse import mybir
from concourse.alu_op_type import AluOpType as ALU

F32, BF16, F16 = mybir.dt.float32, mybir.dt.bfloat16, mybir.dt.float16
ACT = mybir.ActivationFunctionType
AX = mybir.AxisListType

B, S, D = 8, 512, 128
P = 128
NT = S // P
HEADS, HD = 8, 16
TOPK = int(S * 0.2)
SCALE = 0.25 * 1.25
W_LO, W_HI = 25.0, 31.0
E, F = 8, 512
FC = F // P
DI, NS = 256, 16
DC = DI // P
CAP = int(1.2 * 2 * S // E)
LN_EPS = 1e-5
BIG = 1e30
Q_PART = (0, 0, 1, 1, 0, 2, 1, 2)
K_PART = (0, 1, 0, 1, 2, 0, 2, 1)
LOG1P = (0.99999999, -0.49999893, 0.3332971, -0.24951616, 0.19663274, -0.15269667, 0.10543624, -0.05637361,
         0.01954253, -0.00317606)
BIAS = 1024


class Token:

    def __init__(self, sem, value, order):
        self.sem, self.value, self.order = sem, value, order


class Counter:

    def __init__(self, prog, name, eng, sem, unit):
        self.prog, self.name, self.eng, self.sem, self.unit = prog, name, eng, sem, unit
        self.n = BIAS
        self.idle = prog.idle.setdefault(str(eng), None) or prog.ctx.enter_context(prog.nc.semaphore("s_idle_" + name))
        prog.idle[str(eng)] = self.idle

    def at(self, n, back=0):
        v = order = n
        for k, f in enumerate(self.prog.frames):
            step = f["steps"].get(self.name, 0)
            if step:
                v = f["reg"] * step + v
            if back and k == len(self.prog.frames) - 1:
                v = v - step * back
                order = order - step * back
        return Token(self.sem, v, order)

    def last(self):
        return self.at(self.n)

    def did(self, ins):
        ins.then_inc(self.sem, self.unit)
        self.n += self.unit
        return self.at(self.n)

    def after(self, *tokens):
        tokens = sorted((t for t in tokens if t is not None), key=lambda t: t.order)
        tokens = list({id(t.sem): t for t in tokens}.values())
        for t in tokens:
            self.eng.wait_ge(t.sem, t.value)
        if any(not isinstance(t.value, int) for t in tokens):
            self.eng.sem_inc(self.idle, 1)


class Prog:
    def __init__(self, nc, steps, marks):
        self.nc, self.frames, self.steps, self.marks = nc, [], steps, marks
        self.new_steps, self.new_marks = {}, {}
        self.ctx = ExitStack()
        self.counters = {}
        self.idle = {}

    def counter(self, name, eng, unit=1):
        c = Counter(self, name, eng, self.ctx.enter_context(self.nc.semaphore("s_" + name)), unit)
        self.counters[name] = c
        return c

    @contextmanager
    def loop(self, name, trips):
        with self.nc.Fori(0, trips) as reg:
            start = {k: c.n for k, c in self.counters.items()}
            self.frames.append({"reg": reg, "steps": self.steps.get(name, {}), "name": name, "start": start})
            yield reg
            steps = {k: c.n - start[k] for k, c in self.counters.items()}
            self.new_steps[name] = steps
            self.frames.pop()
        for k, c in self.counters.items():
            c.n = start[k] + steps[k] * trips

    def mark(self, name, counter):
        f = self.frames[-1]
        self.new_marks[(f["name"], name)] = counter.n - f["start"][counter.name]

    def carried(self, name, counter):
        f = self.frames[-1]
        off = self.marks.get((f["name"], name), 0)
        return counter.at(f["start"][counter.name] + off, back=1)


def build_program(nc, A, out, steps=None, marks=None, stop=None, nb=B):
    G = Prog(nc, steps or {}, marks or {})
    with G.ctx:
        emit(nc, G, A, out, stop, nb)
    return G.new_steps, G.new_marks


def emit(nc, G, A, out, stop, nb):
    sb = lambda name, shape, dt=F32: G.ctx.enter_context(nc.sbuf_tensor(name, shape, dt))
    ps = lambda name, shape, dt=F32: G.ctx.enter_context(nc.psum_tensor(name, shape, dt))
    pe, act, dve, pool, sp = nc.tensor, nc.scalar, nc.vector, nc.gpsimd, nc.sync
    PE, ACTE, DVE, POOL = (G.counter(n, e) for n, e in (("pe", pe), ("act", act), ("dve", dve), ("pool", pool)))
    LOAD = G.counter("load", sp, 16)
    XIN = G.counter("xin", sp, 16)
    OUT = G.counter("out", sp, 16)
    HOP = G.counter("hop", sp, 16)
    WCP = [G.counter(f"wcp{u}", sp, 16) for u in range(2)]
    WGT = [G.counter(f"wgt{s}", sp, 16) for s in range(2)]
    WGU = [G.counter(f"wgu{s}", sp, 16) for s in range(2)]
    SP = G.counter("sp", sp)
    engines = (PE, ACTE, DVE, POOL)

    def fence():
        marks_ = [c.last() for c in engines]
        for c in engines + (SP,):
            for m in marks_:
                c.after(m)

    for c in G.counters.values():
        c.eng.sem_inc(c.sem, BIAS)
    nc.all_engine_barrier()

    ident = sb("ident", [P, P]); ones_block = sb("ones_block", [P, P])
    onehot = sb("onehot", [32, 32, P], BF16)
    zero_bf = sb("zero_bf", [P, S], BF16)
    iota_rev = sb("iota_rev", [P, NT, E])
    halfs = sb("halfs", [P, NT])
    wts = {}

    def load(name, shape, src):
        wts[name] = sb("w_" + name, shape)
        LOAD.did(sp.dma_start(wts[name][:], src))
        return wts[name]

    for n in ("Wq", "Wk", "Wv", "mix_w", "WoA", "WoB", "Wo"):
        load(n, [P, P], A[n])
    for n in ("bq", "bk", "bv", "bo", "g1", "be1", "g2", "be2", "mix_b", "attn_cb"):
        load(n, [P, 1], A[n])
    load("attn_cw", [P, 3], A["attn_cw"])
    load("router0", [P, E], A["router0"]); load("router1", [P, E], A["router1"])
    load("router1_b", [P, E], A["router1_b"])
    load("b1T", [P, E * FC], A["b1T"]); load("bfcT", [P, E * FC], A["bfcT"]); load("bgT", [P, E * FC], A["bgT"])
    load("b2", [E, D], A["b2"]); load("bproj", [E, D], A["bproj"])
    load("in_projT", [P, 2 * DI], A["in_projT"])
    load("m_cw", [P, DC, 4], A["m_cw"]); load("m_cb", [P, DC], A["m_cb"]); load("m_D", [P, DC], A["m_D"])
    load("x_projT", [P, DC, DI + 2 * NS], A["x_projT"])
    load("dt_projT", [P, DC, DI], A["dt_projT"]); load("dt_b", [P, DC], A["dt_b"])
    load("A_log", [P, DC, NS], A["A_log"])
    load("out_projT", [P, DC, D], A["out_projT"])
    load("cT", [P, 2, B], A["cT"])

    W1 = [sb(f"W1_{s}", [P, F]) for s in range(2)]; W2 = [sb(f"W2_{s}", [P, FC, D]) for s in range(2)]
    WF = [sb(f"WF_{s}", [P, F]) for s in range(2)]; WG = [sb(f"WG_{s}", [P, F]) for s in range(2)]
    WP = [sb(f"WP_{s}", [P, FC, D]) for s in range(2)]

    def load_expert0(s, e):
        WGT[s].did(sp.dma_start(W1[s][:], A["w1"][e])); WGT[s].did(sp.dma_start(W2[s][:], A["w2"][e]))

    def load_expert1(s, e):
        for t, n in ((WF, "wfc"), (WG, "wgate"), (WP, "wproj")):
            WGU[s].did(sp.dma_start(t[s][:], A[n][e]))

    for s in range(2):
        load_expert0(s, s); load_expert1(s, s)

    xr = sb("xr", [P, NT, D])
    nrm = sb("nrm", [P, NT, D]); stats = sb("stats", [P, NT, 6]); mv = sb("mv", [P, NT, 2])
    rstd = sb("rstd", [P, NT]); vpe = sb("vpe", [P, NT])
    hT = sb("hT", [P, S])
    c0 = sb("c0", [P, S]); c1 = sb("c1", [P, S]); c2 = sb("c2", [P, S])
    modT = [sb(f"modT{l}", [P, B, 6]) for l in range(2)]
    mb = sb("mb", [P, 2, 6])
    gbo = sb("gbo", [P, 1]); bo2 = sb("bo2", [P, 1])
    stA = sb("stA", [P, B, 6]); sgn = sb("sgn", [P, B, 6])
    QT = sb("QT", [P, S]); KT = sb("KT", [P, S])
    parts = sb("parts", [P, 3, S], BF16)
    qk = sb("qk", [P, 2, HEADS, S], BF16)
    qs, ks = qk[:, 0], qk[:, 1]
    Vp = sb("Vp", [P, NT, HEADS, 32])
    QW = HEADS * (P + HD)
    Qpad = sb("Qpad", [P, NT, 3, QW], BF16)
    wmask = sb("wmask", [P, NT, HEADS, S], BF16)
    best = sb("best", [P, 13, 8])
    m01 = [sb(f"m01_{i}", [P, S], BF16) for i in range(2)]
    pool_pad = sb("pool_pad", [P, S + 2])
    wj = [sb(f"wj{u}", [P, HEADS, S], BF16) for u in range(2)]
    w_lo = sb("w_lo", [P, S], BF16)
    mx = sb("mx", [P, HEADS]); nmx = sb("nmx", [P, HEADS]); rsum = sb("rsum", [P, HEADS]); rrec = sb("rrec", [P, HEADS])
    rexp = sb("rexp", [P, HEADS, 32]); och = sb("och", [P, 2, P]); ctx_ = sb("ctx", [P, 2, S])
    sm = {n: sb("sm_" + n, [P, NT, E]) for n in ("lg", "p", "t", "oh1", "oh2", "pw1", "pw2", "c")}
    sv = {n: sb("sv_" + n, [P, NT]) for n in ("m", "s", "r", "v1", "v2", "p1", "p2")}
    wjf = [t[0:E].rearrange("p h t -> p (h t)").bitcast(F32) for t in wj]
    CT, OT, WT = (wjf[0][:, n * S:(n + 1) * S] for n in range(3))
    one_row = wjf[1][:, 0:2 * S]
    rows4 = qk[0:E].rearrange("p a h t -> p (a h t)").bitcast(F32).rearrange("p (n c t) -> p n c t", n=4, c=2)
    ohT, pwT, cum, tmpT = (rows4[:, n] for n in range(4))
    cpart = sb("cpart", [32, 3, S], BF16); dpart = sb("dpart", [E, S], BF16); cres = sb("cres", [32, S])
    sil = [sb(f"sil{i}", [P, S]) for i in range(2)]; gat = [sb(f"gat{i}", [P, S]) for i in range(2)]
    hfc = [sb(f"hfc{i}", [P, S]) for i in range(2)]; hg = [sb(f"hg{i}", [P, S]) for i in range(2)]
    cbs = [sb(f"cbs{i}", [P, S]) for i in range(2)]
    junk = c0
    hst = [sb(f"hst{i}", [P, 1]) for i in range(2)]
    yst = sb("yst", [P, E]); ystT = sb("ystT", [E, D])
    xpad = [sb(f"xpad{k}", [P, 3 + S]) for k in range(DC)]
    cols = wmask[:].rearrange("p j h t -> p (j h t)").bitcast(F32).rearrange("p (n k t) -> p n k t", n=8, k=DC)
    xi, sz, din, dl, dtx, yz = (cols[:, n] for n in range(6))
    Aneg = sb("Aneg", [P, DC, NS])
    bB = cbs
    dA, dBx = sil, gat
    hs = hfc; hc = hg
    zc, prob = sil, gat
    pT = [t[:].rearrange("p (a b) -> p a b", b=P) for t in hfc]

    S_ = [ps(f"ps_S{i}", [P, S]) for i in range(2)]
    T_ = [ps(f"ps_T{i}", [P, NT, P]) for i in range(2)]
    Y_ = [ps(f"ps_Y{i}", [P, S]) for i in range(2)]
    M_ = [ps(f"ps_M{i}", [P, S]) for i in range(2)]

    fence()
    for e in (PE, ACTE, DVE, POOL):
        e.after(LOAD.last())
    t = POOL.did(pool.memset(ident[:], 0.0)); POOL.after(t)
    POOL.did(pool.affine_select(out=ident[:], in_=ident[:], compare_op=ALU.not_equal, fill=1.0, base=0,
                                pattern=[[-1, P]], channel_multiplier=1))
    t = POOL.did(pool.memset(onehot[:], 0.0)); POOL.after(t)
    POOL.did(pool.affine_select(out=onehot[:], in_=onehot[:], compare_op=ALU.not_equal, fill=1.0, base=0,
                                pattern=[[-1, 32], [0, P]], channel_multiplier=1))
    t = POOL.did(pool.memset(ones_block[:], 1.0 / (S * W_LO))); POOL.after(t)
    ob = ones_block[:].rearrange("p (g d) -> p g d", d=HD)
    t = POOL.did(pool.affine_select(out=ob, in_=ob, compare_op=ALU.is_ge, fill=0.0, base=0,
                                    pattern=[[-HD, HEADS], [0, HD]], channel_multiplier=1)); POOL.after(t)
    POOL.did(pool.affine_select(out=ob, in_=ob, compare_op=ALU.is_ge, fill=0.0, base=HD - 1,
                                pattern=[[HD, HEADS], [0, HD]], channel_multiplier=-1))
    POOL.did(pool.memset(zero_bf[:], 0.0))
    POOL.did(pool.memset(halfs[:], -0.5))
    POOL.did(pool.memset(w_lo[:], W_LO))
    for e in range(E):
        DVE.did(dve.memset(iota_rev[:, :, e:e + 1], float(E - e)))
    for tz in (Vp, Qpad, pool_pad, xpad[0], xpad[1], rexp):
        DVE.did(dve.memset(tz[:], 0.0))
    ACTE.did(act.activation(wts["cT"][:], wts["cT"][:], ACT.Silu))
    ACTE.did(act.activation(Aneg[:], wts["A_log"][:], ACT.Exp))
    fence()
    DVE.did(dve.tensor_scalar(Aneg[:], Aneg[:], -1.0, None, ALU.mult))
    for l in range(2):
        wm = gat[0]
        for j in range(6):
            fence()
            LOAD.did(sp.dma_start(wm[:, 0:P], A["wmod"][l, :, j * P:(j + 1) * P]))
            PE.after(LOAD.last())
            t = PE.did(pe.matmul(M_[0][:, 0:B], wm[:, 0:P], wts["cT"][:, l, :], start=True, stop=True))
            DVE.after(t)
            DVE.did(dve.tensor_copy(modT[l][:, :, j:j + 1], M_[0][:, 0:B]))
    fence()
    for l in range(2):
        for j in (1, 4):
            DVE.after(DVE.did(dve.tensor_scalar(modT[l][:, :, j:j + 1], modT[l][:, :, j:j + 1], 1.0, None, ALU.add)))
        t = DVE.did(dve.tensor_scalar(sgn[:], modT[l][:], 0.0, 2.0, ALU.is_ge, ALU.mult)); DVE.after(t)
        t = DVE.did(dve.tensor_scalar(sgn[:], sgn[:], 1.0, None, ALU.subtract)); DVE.after(t)
        t = DVE.did(dve.tensor_tensor(stA[:], modT[l][:], sgn[:], ALU.mult)); DVE.after(t)
        t = DVE.did(dve.tensor_scalar(stA[:], stA[:], 0.25, None, ALU.max)); DVE.after(t)
        for j in (2, 5):
            t = DVE.did(dve.tensor_tensor(modT[l][:, :, j:j + 1], stA[:, :, j:j + 1], sgn[:, :, j:j + 1], ALU.mult))
        DVE.after(t)
    t = PE.did(pe.matmul(M_[1][:, 0:1], wts["Wo"][:], wts["bv"][:], start=True, stop=True)); DVE.after(t)
    DVE.did(dve.tensor_tensor(bo2[:], M_[1][:, 0:1], wts["bo"][:], ALU.add))
    DVE.did(dve.tensor_scalar(wts["bq"][:], wts["bq"][:], SCALE, None, ALU.mult))
    fence()

    def layer_norm(src, scale, shift, dst):
        for j in range(NT):
            t = DVE.did(dve.bn_stats(stats[:, j, :], src[:, j, :]))
        DVE.after(t)
        for j in range(NT):
            t = DVE.did(dve.bn_aggr(mv[:, j, :], stats[:, j, :]))
        DVE.after(t)
        t = DVE.did(dve.tensor_scalar(vpe[:], mv[:, :, 1], LN_EPS, None, ALU.add))
        POOL.after(t)
        t = POOL.did(pool.tensor_tensor(rstd[:], vpe[:], halfs[:], ALU.pow))
        DVE.after(t)
        for j in range(NT):
            t = DVE.did(dve.tensor_scalar(nrm[:, j, :], src[:, j, :], mv[:, j, 0:1], rstd[:, j:j + 1],
                                          ALU.subtract, ALU.mult))
            PE.after(t)
            t = PE.did(pe.transpose(T_[0][:, j, :], nrm[:, j, :], ident[:]))
        ACTE.after(t)
        ACTE.did(act.activation(dst[:], T_[0][:].rearrange("p a b -> p (a b)"), ACT.Identity, bias=shift, scale=scale))
        fence()

    def add_to_rows(src):
        for j in range(NT):
            t = PE.did(pe.transpose(T_[1][:, j, :], src[:, j * P:(j + 1) * P], ident[:]))
        DVE.after(t)
        DVE.did(dve.tensor_tensor(xr[:], xr[:], T_[1][:], ALU.add))
        fence()

    def split(src, dst, res):
        t = DVE.did(dve.tensor_copy(dst[:, 0, :], src)); DVE.after(t)
        t = DVE.did(dve.tensor_tensor(res, src, dst[:, 0, :], ALU.subtract)); DVE.after(t)
        t = DVE.did(dve.tensor_copy(dst[:, 1, :], res)); DVE.after(t)
        return DVE.did(dve.tensor_tensor(dst[:, 2, :], res, dst[:, 1, :], ALU.subtract))

    def stack(dst, order):
        for c in engines:
            SP.after(c.last())
        t = HOP.did(sp.dma_start(A["bounce"].rearrange("a p t -> p a t"), parts[:])); SP.after(t)
        for c, part in enumerate(order):
            t = HOP.did(sp.dma_start(dst[c * HD:(c + 1) * HD, :, :], A["bounce"][part].rearrange("(h d) t -> d h t", d=HD)))
        SP.after(t)
        for c in engines:
            c.after(t)

    def close_sum(psum):
        PE.did(pe.matmul(psum[:], zero_bf[:, 0:P], zero_bf[:], start=False, stop=True))

    def attention(b):
        layer_norm(xr, mb[:, 0, 1:2], mb[:, 0, 0:1], hT)
        t = PE.did(pe.matmul(S_[0][:], wts["Wq"][:], hT[:], start=True, stop=True))
        ACTE.after(t)
        ACTE.did(act.activation(QT[:], S_[0][:], ACT.Identity, bias=wts["bq"][:], scale=SCALE))
        t = PE.did(pe.matmul(S_[1][:], wts["Wk"][:], hT[:], start=True, stop=True))
        ACTE.after(t)
        ACTE.did(act.activation(KT[:], S_[1][:], ACT.Identity, bias=wts["bk"][:]))
        for j in range(NT):
            t = PE.did(pe.matmul(M_[0][:, j * P:(j + 1) * P], hT[:, j * P:(j + 1) * P], wts["Wv"][:], start=True, stop=True))
        DVE.after(t)
        for j in range(NT):
            DVE.did(dve.tensor_copy(Vp[:, j, :, 0:HD], M_[0][:, j * P:(j + 1) * P].rearrange("p (h d) -> p h d", d=HD)))
        fence()
        split(KT[:], parts, c0[:])
        stack(ks, K_PART)
        split(QT[:], parts, c0[:])
        stack(qs, Q_PART)
        for j in range(NT):
            t = PE.did(pe.transpose(T_[0][:, j, :], QT[:, j * P:(j + 1) * P], ident[:]))
        DVE.after(t)
        qrow = T_[0][:].rearrange("p j (h d) -> p j h d", d=HD)
        qres = c0[:].rearrange("p (j h d) -> p j h d", j=NT, d=HD)
        pad = [Qpad[:, :, a, :].rearrange("p j (h x) -> p j h x", h=HEADS)[:, :, :, 0:HD] for a in range(3)]
        for j in range(NT):
            t = DVE.did(dve.tensor_copy(pad[0][:, j], qrow[:, j]))
        DVE.after(t)
        for j in range(NT):
            t = DVE.did(dve.tensor_tensor(qres[:, j], qrow[:, j], pad[0][:, j], ALU.subtract))
        DVE.after(t)
        for j in range(NT):
            t = DVE.did(dve.tensor_copy(pad[1][:, j], qres[:, j]))
        DVE.after(t)
        for j in range(NT):
            t = DVE.did(dve.tensor_tensor(pad[2][:, j], qres[:, j], pad[1][:, j], ALU.subtract))
        PE.did(pe.matmul(Y_[0][:], zero_bf[:, 0:P], zero_bf[:], start=True, stop=False))
        fence()
        emphasis(b)
        close_sum(Y_[0])
        fence()
        t = DVE.did(dve.tensor_tensor(c0[:], KT[:], Y_[0][:], ALU.mult)); PE.after(t)
        t = PE.did(pe.matmul(M_[0][:], ones_block[:], c0[:], start=True, stop=True)); ACTE.after(t)
        t = ACTE.did(act.activation(pool_pad[:, 1:S + 1], M_[0][:], ACT.Copy)); DVE.after(t)
        cw = wts["attn_cw"]
        t = DVE.did(dve.tensor_scalar(c0[:], pool_pad[:, 0:S], cw[:, 0:1], wts["attn_cb"][:], ALU.mult, ALU.add)); DVE.after(t)
        t = DVE.did(dve.scalar_tensor_tensor(c1[:], pool_pad[:, 1:S + 1], cw[:, 1:2], c0[:], ALU.mult, ALU.add)); DVE.after(t)
        t = DVE.did(dve.scalar_tensor_tensor(c2[:], pool_pad[:, 2:S + 2], cw[:, 2:3], c1[:], ALU.mult, ALU.add)); DVE.after(t)
        t = DVE.did(dve.tensor_tensor(c1[:], KT[:], c2[:], ALU.mult)); DVE.after(t)
        split(c1[:], parts, c0[:])
        stack(ks, K_PART)
        fence()
        with G.loop("softmax", NT // 2) as j2:
            fence()
            for u in range(2):
                WCP[u].did(sp.dma_start(wj[u][:], wmask[:, bass.ds(j2 * 2 + u, 1)].rearrange("p a h t -> p (a h) t")))
            for u in range(2):
                DVE.after(WCP[u].last())
                softmax_tile(j2 * 2 + u, wj[u])
        fence()
        for k, w in ((0, "WoA"), (1, "WoB")):
            t = PE.did(pe.matmul(M_[0][:], wts[w][:], ctx_[:, k, :], start=k == 0, stop=k == 1))
        ACTE.after(t)
        t = ACTE.did(act.activation(c0[:], M_[0][:], ACT.Identity, bias=gbo[:], scale=mb[:, 0, 2:3]))
        PE.after(t)
        add_to_rows(c0)

    def emphasis(b):
        with G.loop("tiles", NT * HEADS // 2) as i2:
            for u in range(2):
                i = i2 * 2 + u
                h, j = i % HEADS, i // HEADS
                PE.after(G.carried(f"z{u}", ACTE), G.carried(f"m{u}", DVE))
                t = PE.did(pe.matmul(S_[u][:], qs.rearrange("p h t -> p (h t)")[:, bass.ds(h * S + j * P, P)],
                                     ks[:, bass.ds(h, 1), :].rearrange("p a t -> p (a t)"), start=True, stop=True))
                ACTE.after(t, G.carried(f"r{u}", DVE))
                t = ACTE.did(act.activation(zc[u][:], S_[u][:], ACT.Copy)); G.mark(f"z{u}", ACTE)
                DVE.after(t)
                for r in range(13):
                    t = DVE.did(dve.max(best[:, r, :], zc[u][:])); DVE.after(t)
                    if r < 12:
                        t = DVE.did(dve.match_replace(zc[u][:], best[:, r, :], zc[u][:], -BIG)); DVE.after(t)
                G.mark(f"r{u}", DVE)
                DVE.after(G.carried(f"w{u}", POOL))
                rank = TOPK - 96 - 1
                t = DVE.did(dve.tensor_scalar(m01[u][:], S_[u][:], best[:, 12, rank:rank + 1], W_HI - W_LO, ALU.is_ge, ALU.mult)); G.mark(f"m{u}", DVE)
                POOL.after(t)
                wt = wmask[:].rearrange("p j h t -> p (j h) t")[:, bass.ds(i, 1), :].rearrange("p a t -> p (a t)")
                t = POOL.did(pool.tensor_tensor(wt, m01[u][:], w_lo[:], ALU.add)); G.mark(f"w{u}", POOL)
                PE.after(t)
                for a in range(3):
                    PE.did(pe.matmul(Y_[0][:], Qpad[:].rearrange("p j a c -> p (j a c)")[:, bass.ds(j * (3 * QW) + h * P + a * QW, P)],
                                     wt, start=False, stop=False))

    def softmax_tile(j, w):
        jS = j * P
        p_tok = {}
        def scores(h):
            u = h % 2
            PE.after(p_tok.get(("t", h - 2)) if h >= 2 else None)
            t = PE.did(pe.matmul(S_[u][:], qs[:, h, bass.ds(jS, P)], ks[:, h, :], start=True, stop=True))
            DVE.after(t, p_tok.get(("e", h - 2)))
            tt = DVE.did(dve.tensor_tensor_reduce(sil[u][:], S_[u][:], w[:, h, :],
                                                 1.0 / W_LO, -BIG, ALU.mult, ALU.max, mx[:, h:h + 1]))
            p_tok["t", h] = tt
            DVE.after(tt)
            t = DVE.did(dve.tensor_scalar(nmx[:, h:h + 1], mx[:, h:h + 1], -1.0, None, ALU.mult))
            ACTE.after(t, p_tok.get(("x", h - 2)))
            p_tok["e", h] = ACTE.did(act.activation(prob[u][:], sil[u][:], ACT.Exp, bias=nmx[:, h:h + 1], accum_out=rsum[:, h:h + 1]))

        def context(h):
            u = h % 2
            PE.after(p_tok["e", h], p_tok.get(("c", h - 2)))
            for kc in range(NT):
                t = PE.did(pe.transpose(T_[u][:, kc, :], prob[u][:, kc * P:(kc + 1) * P], ident[:]))
            p_tok["x", h] = t
            ACTE.after(t, p_tok.get(("v", h - 2)))
            t = ACTE.did(act.activation(pT[u], T_[u][:], ACT.Copy)); p_tok["c", h] = t
            PE.after(t)
            a, o = h // 4, 32 * (h % 4)
            for kc in range(NT):
                t = PE.did(pe.matmul(Y_[a][o:o + 32, 0:P], Vp[:, kc, h, :], pT[u][:, kc, :], start=kc == 0, stop=kc == NT - 1))
            p_tok["v", h] = t
        fence()
        scores(0)
        for h in range(1, HEADS):
            scores(h)
            context(h - 1)
        context(HEADS - 1)
        t = ACTE.last(); DVE.after(t)
        t = DVE.did(dve.reciprocal(rrec[:], rsum[:])); DVE.after(t)
        for d in range(HD):
            t = DVE.did(dve.tensor_copy(rexp[:, :, d:d + 1], rrec[:].rearrange("p (h a) -> p h a", a=1)))
        PE.after(t)
        for a in range(2):
            t = PE.did(pe.transpose(M_[a][:, 0:P], rexp[:, 4 * a:4 * a + 4, :].rearrange("p h d -> p (h d)"), ident[:]))
        DVE.after(t)
        for a in range(2):
            t = DVE.did(dve.tensor_copy(och[:, a, :], M_[a][:, 0:P]))
        DVE.after(t)
        for a in range(2):
            DVE.did(dve.tensor_tensor(ctx_[:, a, bass.ds(jS, P)], Y_[a][:, 0:P], och[:, a, :], ALU.mult))

    def bcast(v):
        return v[:].rearrange("p (j a) -> p j a", a=1).broadcast_to([P, NT, E])

    def first_max(src, oh, vmax, scratch):
        t = DVE.did(dve.tensor_reduce(vmax[:], src[:], AX.X, ALU.max)); DVE.after(t)
        t = DVE.did(dve.tensor_tensor(scratch[:], src[:], bcast(vmax), ALU.is_equal)); DVE.after(t)
        t = DVE.did(dve.tensor_tensor(scratch[:], scratch[:], iota_rev[:], ALU.mult)); DVE.after(t)
        t = DVE.did(dve.tensor_reduce(sv["m"][:], scratch[:], AX.X, ALU.max)); DVE.after(t)
        t = DVE.did(dve.tensor_tensor(oh[:], scratch[:], bcast(sv["m"]), ALU.is_equal)); DVE.after(t)

    def rows_to_experts(src, dst):
        PE.after(DVE.last(), ACTE.last())
        for j in range(NT):
            t = PE.did(pe.transpose(T_[1][0:E, j, :], src[:, j, :], ident[:]))
        DVE.after(t)
        t = DVE.did(dve.tensor_copy(dst, T_[1][0:E].rearrange("e j t -> e (j t)")))
        DVE.after(t)

    def router(w):
        PE.after(DVE.last(), ACTE.last())
        for j in range(NT):
            t = PE.did(pe.matmul(M_[0][:, j * E:(j + 1) * E], hT[:, j * P:(j + 1) * P], wts[w][:], start=True, stop=True))
        DVE.after(t)
        return M_[0][:, 0:NT * E].rearrange("p (j e) -> p j e", e=E)

    def mixture0(b):
        layer_norm(xr, mb[:, 0, 4:5], mb[:, 0, 3:4], c1)
        for j in range(NT):
            t = PE.did(pe.transpose(T_[1][:, j, :], c1[:, j * P:(j + 1) * P], ident[:]))
        DVE.after(t)
        layer_norm(T_[1], wts["g1"][:], wts["be1"][:], c0)
        t = PE.did(pe.matmul(M_[0][:], wts["mix_w"][:], c0[:], start=True, stop=True)); DVE.after(t)
        t = DVE.did(dve.scalar_tensor_tensor(c2[:], M_[0][:], wts["mix_b"][:], c0[:], ALU.add, ALU.add)); DVE.after(t)
        t = DVE.did(dve.tensor_tensor(c2[:], c2[:], c1[:], ALU.add)); PE.after(t)
        for j in range(NT):
            t = PE.did(pe.transpose(T_[1][:, j, :], c2[:, j * P:(j + 1) * P], ident[:]))
        DVE.after(t)
        layer_norm(T_[1], wts["g2"][:], wts["be2"][:], hT)
        lg = router("router0")
        t = DVE.did(dve.tensor_reduce(sv["m"][:], lg, AX.X, ALU.max)); DVE.after(t)
        t = DVE.did(dve.tensor_tensor(sm["t"][:], lg, bcast(sv["m"]), ALU.subtract)); ACTE.after(t)
        t = ACTE.did(act.activation(sm["p"][:], sm["t"][:], ACT.Exp)); DVE.after(t)
        t = DVE.did(dve.tensor_reduce(sv["s"][:], sm["p"][:], AX.X, ALU.add)); DVE.after(t)
        t = DVE.did(dve.reciprocal(sv["r"][:], sv["s"][:])); DVE.after(t)
        t = DVE.did(dve.tensor_tensor(sm["p"][:], sm["p"][:], bcast(sv["r"]), ALU.mult)); DVE.after(t)
        first_max(sm["p"], sm["oh1"], sv["v1"], sm["t"])
        t = DVE.did(dve.tensor_tensor(sm["lg"][:], sm["p"][:], sm["oh1"][:], ALU.subtract)); DVE.after(t)
        first_max(sm["lg"], sm["oh2"], sv["v2"], sm["t"])
        t = DVE.did(dve.tensor_tensor(sm["t"][:], sm["oh1"][:], sm["oh2"][:], ALU.add)); DVE.after(t)
        t = DVE.did(dve.tensor_tensor(sm["c"][:], sm["t"][:], sm["p"][:], ALU.mult)); DVE.after(t)
        rows_to_experts(sm["c"], CT)
        split(CT, cpart[0:E], cres[0:E])
        fence()
        PE.did(pe.matmul(Y_[0][:], wts["b2"][:], CT, start=True, stop=False))
        fence()
        with G.loop("pairs0", E // 2) as e2:
            experts0(e2)
        close_sum(Y_[0])
        fence()
        t = DVE.did(dve.tensor_tensor(c0[:], Y_[0][:], c2[:], ALU.add)); DVE.after(t)
        t = DVE.did(dve.tensor_scalar(c0[:], c0[:], mb[:, 0, 5:6], None, ALU.mult)); PE.after(t)
        add_to_rows(c0)

    def experts0(e2):
        seq = [(s, c) for s in range(2) for c in range(FC)]
        tk = {}
        PE.after(DVE.last(), ACTE.last())
        ACTE.after(DVE.last(), PE.last()); DVE.after(PE.last())
        def up(n):
            s, c = seq[n]
            if c == 0:
                for a in range(3):
                    if a == 0:
                        PE.after(tk.get(("w", n - 1)))
                    t = PE.did(pe.matmul(M_[s][:], onehot[0:E, bass.ds(e2 * 2 + s, 1), :].rearrange("e a p -> e (a p)"), cpart[0:E, a, :], start=a == 0, stop=a == 2))
                tk["cb", s] = t
                PE.after(WGT[s].last())
            PE.after(tk.get(("a", n - 2)))
            t = PE.did(pe.matmul(S_[n % 2][:], W1[s][:, c * P:(c + 1) * P], hT[:], start=True, stop=True))
            ACTE.after(t, tk.get(("w", n - 2)))
            t = ACTE.did(act.activation(sil[n % 2][:], S_[n % 2][:], ACT.Silu, bias=wts["b1T"][:, bass.ds(e2 * (2 * FC) + s * FC + c, 1)]))
            tk["a", n] = t
            DVE.after(t, tk["cb", s], tk.get(("y", n - 2)))
            tk["w", n] = DVE.did(dve.tensor_tensor(gat[n % 2][:], sil[n % 2][:], M_[s][:], ALU.mult))

        def down(n):
            s, c = seq[n]
            PE.after(tk["w", n])
            tk["y", n] = PE.did(pe.matmul(Y_[0][:], W2[s][:, c, :], gat[n % 2][:], start=False, stop=False))
            if c == FC - 1:
                SP.after(tk["y", n])
                load_expert0(s, bass.ds(e2 * 2 + (2 + s), 1))
        up(0)
        for n in range(1, len(seq)):
            up(n)
            down(n - 1)
        down(len(seq) - 1)

    def mamba(b):
        layer_norm(xr, mb[:, 1, 1:2], mb[:, 1, 0:1], hT)
        for k in range(2 * DC):
            ps_ = S_[k % 2]
            PE.after(ACTE.last())
            t = PE.did(pe.matmul(ps_[:], wts["in_projT"][:, k * P:(k + 1) * P], hT[:], start=True, stop=True))
            ACTE.after(t)
            if k < DC:
                ACTE.did(act.activation(xpad[k][:, 3:3 + S], ps_[:], ACT.Copy))
            else:
                ACTE.did(act.activation(sz[:, k - DC, :], ps_[:], ACT.Silu))
        fence()
        for k in range(DC):
            cw = wts["m_cw"][:, k, :]
            t = DVE.did(dve.tensor_scalar(c0[:], xpad[k][:, 0:S], cw[:, 0:1], None, ALU.mult)); DVE.after(t)
            t = DVE.did(dve.scalar_tensor_tensor(c1[:], xpad[k][:, 1:1 + S], cw[:, 1:2], c0[:], ALU.mult, ALU.add)); DVE.after(t)
            t = DVE.did(dve.scalar_tensor_tensor(c0[:], xpad[k][:, 2:2 + S], cw[:, 2:3], c1[:], ALU.mult, ALU.add)); DVE.after(t)
            t = DVE.did(dve.scalar_tensor_tensor(c1[:], xpad[k][:, 3:3 + S], cw[:, 3:4], c0[:], ALU.mult, ALU.add)); ACTE.after(t)
            t = ACTE.did(act.activation(xi[:, k, :], c1[:], ACT.Silu, bias=wts["m_cb"][:, k:k + 1])); DVE.after(t)
        fence()
        for m in range(DC):
            for k in range(DC):
                t = PE.did(pe.matmul(S_[m][:], wts["x_projT"][:, k, m * P:(m + 1) * P], xi[:, k, :], start=k == 0, stop=k == DC - 1))
            ACTE.after(t)
            ACTE.did(act.activation(din[:, m, :], S_[m][:], ACT.Copy))
        for k in range(DC):
            t = PE.did(pe.matmul(M_[0][0:2 * NS, :], wts["x_projT"][:, k, DI:DI + 2 * NS], xi[:, k, :], start=k == 0, stop=k == DC - 1))
        DVE.after(t)
        split(M_[0][0:2 * NS, :], cpart, cres[:])
        fence()
        for m in range(DC):
            for k in range(DC):
                t = PE.did(pe.matmul(S_[m][:], wts["dt_projT"][:, k, m * P:(m + 1) * P], din[:, k, :], start=k == 0, stop=k == DC - 1))
            DVE.after(t)
            DVE.did(dve.tensor_scalar(yz[:, m, :], S_[m][:], wts["dt_b"][:, m:m + 1], None, ALU.add))
            PE.did(pe.matmul(Y_[m][:], zero_bf[:, 0:P], zero_bf[:], start=True, stop=False))
        t = DVE.last(); DVE.after(t)
        v, e, q = (w.rearrange("p k t -> p (k t)") for w in (yz, dtx, din))
        t = DVE.did(dve.scalar_tensor_tensor(e, v, -1.0, v, ALU.mult, ALU.max)); ACTE.after(t)
        t = ACTE.did(act.activation(e, e, ACT.Exp, scale=-1.0)); DVE.after(t)
        t = DVE.did(dve.tensor_scalar(q, e, LOG1P[-1], None, ALU.mult)); DVE.after(t)
        for coef in LOG1P[-2::-1]:
            t = DVE.did(dve.scalar_tensor_tensor(q, q, coef, e, ALU.add, ALU.mult)); DVE.after(t)
        t = DVE.did(dve.scalar_tensor_tensor(dl.rearrange("p k t -> p (k t)"), v, 0.0, q, ALU.max, ALU.add)); DVE.after(t)
        DVE.did(dve.tensor_tensor(dtx, dl, xi, ALU.mult))
        fence()
        with G.loop("states", NS // 2) as s2:
            for u in range(2):
                state(s2 * 2 + u, u)
        for k in range(DC):
            close_sum(Y_[k])
        fence()
        for k in range(DC):
            t = DVE.did(dve.scalar_tensor_tensor(c0[:], xi[:, k, :], wts["m_D"][:, k:k + 1], Y_[k][:], ALU.mult, ALU.add)); DVE.after(t)
            t = DVE.did(dve.tensor_tensor(yz[:, k, :], c0[:], sz[:, k, :], ALU.mult)); DVE.after(t); PE.after(t)
            t = PE.did(pe.matmul(M_[0][:], wts["out_projT"][:, k, :], yz[:, k, :], start=k == 0, stop=k == DC - 1))
        ACTE.after(t)
        t = ACTE.did(act.activation(c0[:], M_[0][:], ACT.Copy, scale=mb[:, 1, 2:3])); PE.after(t)
        add_to_rows(c0)

    def state(s, u):
        for v, psum in ((0, S_[u]), (1, M_[u])):
            PE.after(G.carried(f"B{u}", ACTE) if v == 0 else G.carried(f"C{u}", DVE))
            for a in range(3):
                t = PE.did(pe.matmul(psum[:], onehot[:, bass.ds(s + v * NS, 1), :].rearrange("e a p -> e (a p)"), cpart[:, a, :], start=a == 0, stop=a == 2))
            if v == 0:
                ACTE.after(t, G.carried(f"x{u}", POOL))
                tb = ACTE.did(act.activation(bB[u][:], psum[:], ACT.Copy)); G.mark(f"B{u}", ACTE)
            else:
                tc = t
        for k in range(DC):
            ACTE.after(G.carried(f"s{k}", DVE))
            if (u, k) in chain:
                ACTE.after(chain[u, k])
            ta = ACTE.did(act.activation(dA[k][:], dl[:, k, :], ACT.Exp, scale=Aneg[:, k, bass.ds(s, 1)]))
            POOL.after(tb, G.carried(f"s{k}", DVE), chain.get((u, k)))
            tx = POOL.did(pool.tensor_tensor(dBx[k][:], dtx[:, k, :], bB[u][:], ALU.mult))
            DVE.after(ta, tx)
            t = DVE.did(dve.tensor_tensor_scan(hs[k][:], dA[k][:], dBx[k][:], 0.0, ALU.mult, ALU.add))
            G.mark(f"s{k}", DVE)
            chain[u + 1, k] = t
            DVE.after(t, tc, chain.get(("y", u, k)), G.carried(f"y{k}", PE))
            t = DVE.did(dve.tensor_tensor(hc[k][:], hs[k][:], M_[u][:], ALU.mult))
            PE.after(t)
            t = PE.did(pe.matmul(Y_[k][:], ident[:], hc[k][:], start=False, stop=False))
            G.mark(f"y{k}", PE)
            chain["y", u + 1, k] = t
        G.mark(f"C{u}", DVE); G.mark(f"x{u}", POOL)
        if u == 1:
            chain.clear()

    chain = {}

    def mixture1(b):
        layer_norm(xr, mb[:, 1, 4:5], mb[:, 1, 3:4], hT)
        lg_ps = router("router1")
        t = DVE.did(dve.tensor_tensor(sm["lg"][:], lg_ps, wts["router1_b"][:].rearrange("p (a e) -> p a e", a=1).broadcast_to([P, NT, E]), ALU.add)); DVE.after(t)
        first_max(sm["lg"], sm["oh1"], sv["v1"], sm["t"])
        t = DVE.did(dve.scalar_tensor_tensor(sm["p"][:], sm["oh1"][:], -BIG, sm["lg"][:], ALU.mult, ALU.add)); DVE.after(t)
        first_max(sm["p"], sm["oh2"], sv["v2"], sm["t"])
        t = DVE.did(dve.tensor_tensor(sv["s"][:], sv["v2"][:], sv["v1"][:], ALU.subtract)); ACTE.after(t)
        t = ACTE.did(act.activation(sv["r"][:], sv["s"][:], ACT.Exp)); DVE.after(t)
        t = DVE.did(dve.tensor_scalar(sv["s"][:], sv["r"][:], 1.0, None, ALU.add)); DVE.after(t)
        t = DVE.did(dve.reciprocal(sv["p1"][:], sv["s"][:])); DVE.after(t)
        t = DVE.did(dve.tensor_tensor(sv["p2"][:], sv["p1"][:], sv["r"][:], ALU.mult)); DVE.after(t)
        DVE.did(dve.tensor_tensor(sm["pw1"][:], sm["oh1"][:], bcast(sv["p1"]), ALU.mult))
        t = DVE.did(dve.tensor_tensor(sm["pw2"][:], sm["oh2"][:], bcast(sv["p2"]), ALU.mult)); DVE.after(t)
        rows_to_experts(sm["oh1"], ohT[:, 0, :]); rows_to_experts(sm["oh2"], ohT[:, 1, :])
        rows_to_experts(sm["pw1"], pwT[:, 0, :]); rows_to_experts(sm["pw2"], pwT[:, 1, :])
        t = DVE.did(dve.memset(one_row, 1.0)); DVE.after(t)
        fl = lambda v: v.rearrange("e c t -> e (c t)")
        t = DVE.did(dve.tensor_tensor_scan(fl(cum), one_row, fl(ohT), 0.0, ALU.mult, ALU.add)); DVE.after(t)
        for dst, test, what in ((CT, ALU.is_le, pwT), (OT, ALU.is_gt, pwT), (dpart, ALU.is_equal, ohT)):
            t = DVE.did(dve.scalar_tensor_tensor(fl(tmpT), fl(cum), float(CAP), fl(what), test, ALU.mult)); DVE.after(t)
            t = DVE.did(dve.tensor_tensor(dst[:], tmpT[:, 0, :], tmpT[:, 1, :], ALU.add)); DVE.after(t)
        t = DVE.did(dve.tensor_tensor(WT, pwT[:, 0, :], pwT[:, 1, :], ALU.add)); DVE.after(t)
        split(CT, cpart[0:E], cres[0:E])
        fence()
        PE.did(pe.matmul(Y_[0][:], wts["bproj"][:], WT, start=True, stop=False))
        fence()
        with G.loop("pairs1", E // 2) as e2:
            experts1(e2)
        fence()
        t = DVE.did(dve.tensor_copy(yst[:], M_[1][:, 0:E])); PE.after(t)
        t = PE.did(pe.transpose(T_[1][0:E, 0, :], yst[:], ident[:])); DVE.after(t)
        t = DVE.did(dve.tensor_copy(ystT[:], T_[1][0:E, 0, :])); PE.after(t)
        t = PE.did(pe.matmul(Y_[0][:], ystT[:], OT, start=False, stop=True)); DVE.after(t)
        t = DVE.did(dve.tensor_scalar(c0[:], Y_[0][:], mb[:, 1, 5:6], None, ALU.mult)); PE.after(t)
        add_to_rows(c0)

    def experts1(e2):
        seq = [(s, c) for s in range(2) for c in range(FC)]
        tk = {}
        fence()
        T0 = T_[0][:].rearrange("p a b -> p (a b)"); T1 = T_[1][:].rearrange("p a b -> p (a b)")
        def up(n):
            s, c = seq[n]
            col = e2 * (2 * FC) + s * FC + c
            sel = onehot[0:E, bass.ds(e2 * 2 + s, 1), :].rearrange("e a p -> e (a p)")
            u = n % 2
            if c == 0:
                PE.after(tk.get("cb"))
                for a in range(3):
                    t = PE.did(pe.matmul(M_[0][:], sel, cpart[0:E, a, :], start=a == 0, stop=a == 2))
                ACTE.after(t, tk.get(("w", n - 1)))
                tk["cb"] = ACTE.did(act.activation(cbs[0][:], M_[0][:], ACT.Copy))
                PE.after(tk["cb"])
                t = PE.did(pe.matmul(M_[0][:], sel, dpart[:], start=True, stop=True))
                ACTE.after(t)
                tk["cb"] = ACTE.did(act.activation(cbs[1][:], M_[0][:], ACT.Copy))
                PE.after(WGU[s].last())
            PE.after(tk.get(("a", n - 2)))
            t = PE.did(pe.matmul(S_[u][:], WF[s][:, c * P:(c + 1) * P], hT[:], start=True, stop=True))
            ACTE.after(t, tk.get(("g", n - 2)))
            th = ACTE.did(act.activation(hfc[u][:], S_[u][:], ACT.Identity, bias=wts["bfcT"][:, bass.ds(col, 1)]))
            tk["a", n] = th
            PE.after(tk.get(("g", n - 2)))
            t = PE.did(pe.matmul((T0, T1)[u], WG[s][:, c * P:(c + 1) * P], hT[:], start=True, stop=True))
            DVE.after(t, th, tk.get(("s", n - 2)))
            t = DVE.did(dve.scalar_tensor_tensor(hg[u][:], (T0, T1)[u], wts["bgT"][:, bass.ds(col, 1)], hfc[u][:], ALU.add, ALU.mult))
            tk["g", n] = t
            ACTE.after(t, tk.get(("w", n - 2)))
            t = ACTE.did(act.activation(sil[u][:], hg[u][:], ACT.Silu)); tk["s", n] = t
            DVE.after(t, tk["cb"], tk.get(("y", n - 2)))
            DVE.did(dve.tensor_tensor(gat[u][:], sil[u][:], cbs[0][:], ALU.mult))
            DVE.after(tk.get(("w", n - 1)))
            tk["w", n] = DVE.did(dve.tensor_tensor_reduce(junk[:], sil[u][:], cbs[1][:], 1.0, 0.0, ALU.mult, ALU.add, hst[u][:]))

        def down(n):
            s, c = seq[n]
            PE.after(tk["w", n])
            PE.did(pe.matmul(Y_[0][:], WP[s][:, c, :], gat[n % 2][:], start=False, stop=False))
            tk["y", n] = PE.did(pe.matmul(M_[1][:, bass.ds(e2 * 2 + s, 1)], WP[s][:, c, :], hst[n % 2][:], start=c == 0, stop=c == FC - 1))
            if c == FC - 1:
                SP.after(tk["y", n])
                load_expert1(s, bass.ds(e2 * 2 + (2 + s), 1))
        up(0)
        for n in range(1, len(seq)):
            up(n)
            down(n - 1)
        down(len(seq) - 1)

    with G.loop("batch", nb) as b:
        SP.after(*[c.last() for c in engines], OUT.last())
        t = XIN.did(sp.dma_start(xr[:], A["x"][bass.ds(b, 1)].rearrange("a (j p) d -> p (a j) d", p=P)))
        DVE.after(t)
        for l in range(2):
            DVE.did(dve.tensor_copy(mb[:, l, :], modT[l][:, bass.ds(b, 1), :]))
        t = DVE.last(); DVE.after(t)
        DVE.did(dve.tensor_tensor(gbo[:], bo2[:], mb[:, 0, 2:3], ALU.mult))
        fence()
        attention(b)
        if stop == "attn":
            pass
        else:
            mixture0(b)
            if stop != "moe0":
                mamba(b)
                if stop != "mamba":
                    mixture1(b)
        SP.after(*[c.last() for c in engines])
        OUT.did(sp.dma_start(out[bass.ds(b, 1)].rearrange("a (j p) d -> p (a j) d", p=P), xr[:]))
    for c in (OUT, XIN, HOP, LOAD, *WGT, *WGU):
        SP.after(c.last())
    for c in engines:
        SP.after(c.last())


def kernel(**inputs):
    import concourse.bacc as bacc
    from concourse.bass_utils import run_bass_kernel_spmd

    a = {k: np.asarray(v) for k, v in inputs.items()}
    col = lambda v: np.ascontiguousarray(v.reshape(P, 1))
    chunks = lambda v, n: np.ascontiguousarray(v.reshape(n, P, *v.shape[1:]).swapaxes(0, 1))
    again = lambda v: np.concatenate([v, v[:2]])
    wo = a["L0_attn_Wo"].reshape(2, 4, HD, D)
    padded = np.zeros((2, 4, 2, HD, D), np.float32)
    padded[:, :, 0] = wo
    padded = padded.reshape(2, P, D)
    data = {
        "x": a["L0_attn_x"], "Wq": a["L0_attn_Wq"], "Wk": a["L0_attn_Wk"], "Wv": a["L0_attn_Wv"], "Wo": a["L0_attn_Wo"],
        "WoA": padded[0], "WoB": padded[1], "mix_w": a["L0_ffn_mix_w"],
        "bq": col(a["L0_attn_bq"]), "bk": col(a["L0_attn_bk"]), "bv": col(a["L0_attn_bv"]), "bo": col(a["L0_attn_bo"]),
        "g1": col(a["L0_ffn_g1"]), "be1": col(a["L0_ffn_be1"]), "g2": col(a["L0_ffn_g2"]), "be2": col(a["L0_ffn_be2"]),
        "mix_b": col(a["L0_ffn_mix_b"]),
        "attn_cw": np.repeat(a["L0_attn_conv_w"][:, 0, :], HD, axis=0), "attn_cb": np.repeat(a["L0_attn_conv_b"], HD).reshape(P, 1),
        "router0": a["L0_ffn_router_w"], "router1": a["L1_ffn_router_w"],
        "router1_b": np.repeat(a["L1_ffn_router_b"].reshape(1, E), P, axis=0),
        "b1T": a["L0_ffn_b1"].reshape(E * FC, P).T, "b2": a["L0_ffn_b2"],
        "bfcT": a["L1_ffn_b_c_fc"].reshape(E * FC, P).T, "bgT": a["L1_ffn_b_gate"].reshape(E * FC, P).T,
        "bproj": a["L1_ffn_b_c_proj"].reshape(E, D),
        "in_projT": a["L1_attn_in_proj_w"].T, "m_cw": chunks(a["L1_attn_conv_w"][:, 0, :], DC),
        "m_cb": a["L1_attn_conv_b"].reshape(DC, P).T, "m_D": a["L1_attn_D"].reshape(DC, P).T,
        "x_projT": chunks(a["L1_attn_x_proj_w"].T, DC), "dt_projT": chunks(a["L1_attn_dt_proj_w"].T, DC),
        "dt_b": a["L1_attn_dt_proj_b"].reshape(DC, P).T, "A_log": chunks(a["L1_attn_A_log"], DC),
        "out_projT": chunks(a["L1_attn_out_proj_w"].T, DC),
        "cT": np.stack([a["L0_c"].T, a["L1_c"].T], axis=1), "wmod": np.stack([a["L0_wmod"], a["L1_wmod"]]),
        "w1": again(a["L0_ffn_w1"]), "w2": again(a["L0_ffn_w2"].reshape(E, FC, P, D).swapaxes(1, 2)),
        "wfc": again(a["L1_ffn_w_c_fc"]), "wgate": again(a["L1_ffn_w_gate"]),
        "wproj": again(a["L1_ffn_w_c_proj"].reshape(E, FC, P, D).swapaxes(1, 2)),
    }
    data = {k: np.ascontiguousarray(v) for k, v in data.items()}

    def built(steps, marks):
        nc = bacc.Bacc("TRN2", target_bir_lowering=False, num_devices=1)
        aps = {k: nc.dram_tensor("in_" + k, v.shape, mybir.dt.from_np(v.dtype), kind="ExternalInput").ap() for k, v in data.items()}
        aps["bounce"] = nc.dram_tensor("bounce", (3, P, S), BF16, kind="Internal").ap()
        out = nc.dram_tensor("out", (B, S, D), F32, kind="ExternalOutput").ap()
        return nc, build_program(nc, aps, out, steps, marks)

    _, (steps, marks) = built(None, None)
    nc, _ = built(steps, marks)
    r = run_bass_kernel_spmd(nc, [{"in_" + k: v for k, v in data.items()}], core_ids=[0])
    return r.results[0]["out"]
```
